# Optimizing a Trainium2 kernel written in Bass

```python
import numpy as np
import jax
import jax.numpy as jnp

def _softmax(x, axis=-1):
    return jax.nn.softmax(x, axis=axis)
def _gelu(x):
    return jax.nn.gelu(x, approximate=True)
def _silu(x):
    return jax.nn.silu(x)
def _sigmoid(x):
    return jax.nn.sigmoid(x)
def _layernorm(x, axis=-1, eps=1e-5):
    m = jnp.mean(x, axis=axis, keepdims=True)
    v = jnp.var(x, axis=axis, keepdims=True)
    return (x - m) / jnp.sqrt(v + eps)
def _scatter_add(tgt, idx, src, axis=0):
    return tgt.at[idx].add(src)
def _segment_sum(src, seg, n):
    return jax.ops.segment_sum(src, seg, n)

kernel_name = 'mk_conv_preact_d1_conv_nhwc128_34a615'

def setup_inputs(seed: int = 0):
    np.random.seed(seed)
    _w = jnp.asarray
    def _rec_inputs():
        import jax
        import jax.numpy as jnp
        _gk = jax.random.key(seed)
        x = -1.904e-05 + 0.9999 * jax.random.normal(jax.random.fold_in(_gk, 1), (8, 200, 288, 128), jnp.float32)
        return x
    x = _rec_inputs()
    def _L0_conv_setup():
        import jax, jax.numpy as jnp
        import numpy as np
        B, N, L, D, K = (8, 200, 288, 128, 128)
        key = jax.random.key(seed)
        ks = jax.random.split(key, 6)
        s = 1.0 / np.sqrt(D)
        return {'X': jax.random.normal(ks[0], (B, N, L, D), dtype=jnp.float32), 'pattern': jax.random.normal(ks[1], (K, D), dtype=jnp.float32), 'Wq': jax.random.normal(ks[2], (D, D), dtype=jnp.float32) * s, 'bq': jax.random.normal(ks[3], (D,), dtype=jnp.float32) * s, 'Wk': jax.random.normal(ks[4], (D, D), dtype=jnp.float32) * s, 'bk': jax.random.normal(ks[5], (D,), dtype=jnp.float32) * s}
    _L0_conv_all = _L0_conv_setup()
    _L0_conv_in = {k: v for k, v in _L0_conv_all.items() if k in ('pattern', 'Wq', 'bq', 'Wk', 'bk', )}
    del _L0_conv_all

    return {
        "x": x,
        "L0_conv_pattern": _L0_conv_in["pattern"],
        "L0_conv_Wq": _L0_conv_in["Wq"],
        "L0_conv_bq": _L0_conv_in["bq"],
        "L0_conv_Wk": _L0_conv_in["Wk"],
        "L0_conv_bk": _L0_conv_in["bk"],
    }

def reference(x, L0_conv_pattern, L0_conv_Wq, L0_conv_bq, L0_conv_Wk, L0_conv_bk):
    import jax
    import jax.numpy as jnp
    def _L0_conv_ref(X, pattern, Wq, bq, Wk, bk):
        import jax, jax.numpy as jnp
        import numpy as np
        B, N, L, D, K = (8, 200, 288, 128, 128)
        pat_k = pattern @ Wk.T + bk
        qry = jnp.einsum('bnld,ed->bnle', X, Wq) + bq
        temperature = jnp.sqrt(jnp.asarray(D, dtype=X.dtype))
        weight = jnp.einsum('kd,bnld->bnlk', pat_k, qry) / temperature
        weight = jax.nn.softmax(weight, axis=3)
        w_X = jnp.einsum('bnlk,kd->bnld', weight, pattern)
        return w_X

    def _gn(v, G=32, eps=1e-5):
        B_, H_, W_, C_ = v.shape
        g = v.reshape(B_, H_, W_, G, C_ // G)
        m = jnp.mean(g, axis=(1, 2, 4), keepdims=True)
        s = jnp.var(g, axis=(1, 2, 4), keepdims=True)
        return ((g - m) / jnp.sqrt(s + eps)).reshape(v.shape)

    def _ln_c(v, eps=1e-6):
        m = jnp.mean(v, axis=-1, keepdims=True)
        s = jnp.var(v, axis=-1, keepdims=True)
        return (v - m) / jnp.sqrt(s + eps)

    def _ln_t(v, eps=1e-5):
        m = jnp.mean(v, axis=-1, keepdims=True)
        s = jnp.var(v, axis=-1, keepdims=True)
        return (v - m) / jnp.sqrt(s + eps)

    def _to_tokens(v):
        B_, H_, W_, C_ = v.shape
        return v.reshape(B_, H_ * W_, C_)
    def _from_tokens(t, like):
        return t.reshape(like.shape)

    x = x + _L0_conv_ref(_gn(x), L0_conv_pattern, L0_conv_Wq, L0_conv_bq, L0_conv_Wk, L0_conv_bk)
    return x


_drawn_inputs = setup_inputs


def setup_inputs(seed=0):
    import zlib

    import numpy as np

    out = dict(_drawn_inputs(seed))
    spreads = {}
    factors = {'L0_conv_bq': 4.64, 'L0_conv_bk': 8.0}
    for name, (base, spread) in spreads.items():
        noise = np.random.default_rng([zlib.crc32(name.encode()), seed]).standard_normal(out[name].shape)
        drawn = base * np.exp(spread * noise) if base else spread * noise
        out[name] = jnp.asarray(drawn.astype(out[name].dtype))
    for name, factor in factors.items():
        out[name] = (out[name] * factor).astype(out[name].dtype)
    return out
```

```python
from contextlib import ExitStack

import concourse.bass as bass
from concourse import mybir

ALU = mybir.AluOpType
ACT = mybir.ActivationFunctionType
F32 = mybir.dt.float32
BF16 = mybir.dt.bfloat16
AX_X = mybir.AxisListType.X

P = 128
TILES = 3
GROUP_CHUNK = 3
CHUNK_T = TILES * GROUP_CHUNK
CHUNKS = 10
BODY = GROUP_CHUNK * CHUNKS
SLAB_T = CHUNK_T * CHUNKS
NG = 32
EPS = 1e-5
SLAB_STEPS = 7
XBUFS = 5
OBUFS = 5
RING = 3
BANKS = 2
LEAD = 4


def program(nc, x, pattern, Wq, bq, Wk, bk, out):
    B, H, W_, C = x.shape
    K = pattern.shape[0]
    assert C == P and K == P
    tokens = H * W_
    batch_t = tokens // P
    bodies = batch_t // SLAB_T
    assert tokens == P * batch_t and batch_t == bodies * SLAB_T
    all_bodies = B * bodies
    last_lag = 4
    CW = C // NG
    W1 = C + 1
    inv_sqrt_d = float(C) ** -0.5
    half_count = SLAB_T * CW // 2
    means = bodies * 2

    x_chunks = x.rearrange("b h w c -> (b h w c)").rearrange("(n p f) -> n p f", p=P, f=CHUNK_T * C)
    out_chunks = out.rearrange("b h w c -> (b h w c)").rearrange("(n p f) -> n p f", p=P, f=CHUNK_T * C)

    with ExitStack() as ctx:
        def sb(name, shape, dt=F32):
            return ctx.enter_context(nc.sbuf_tensor(name, shape, dt))

        def sem(name):
            return ctx.enter_context(nc.semaphore(name))

        slab = sb("slab", [P, 2, SLAB_T * C])
        x_sb = sb("x_sb", [P, XBUFS, CHUNK_T * C])
        out_sb = sb("out_sb", [P, OBUFS, CHUNK_T * C])
        xT_sb = sb("xT_sb", [P, RING, TILES * P])
        shift_sb = sb("shift_sb", [P, RING, TILES * K])
        prob_sb = sb("prob_sb", [P, RING, TILES * P])
        y_sb = sb("y_sb", [P, RING, TILES * C])
        negmax = sb("negmax", [P, RING, TILES])
        rsum = sb("rsum", [P, RING, TILES])
        ident = sb("ident", [P, P])
        mean_w = sb("mean_w", [P, P])
        ones_bf = sb("ones_bf", [P, P], BF16)
        bias_bf = sb("bias_bf", [P, K], BF16)
        pat_aug = sb("pat_aug", [P, W1])
        Wq_sb = sb("Wq_sb", [P, C])
        Wk_sb = sb("Wk_sb", [P, C])
        bq_sb = sb("bq_sb", [P, 1])
        bk_sb = sb("bk_sb", [P, 1])
        WkT_sb = sb("WkT_sb", [P, P])
        patT_sb = sb("patT_sb", [P, P])
        patkT_sb = sb("patkT_sb", [P, K])
        A_sb = sb("A_sb", [P, K])
        bias_c = sb("bias_c", [P, K])
        M_sb = sb("M_sb", [P, K])
        stats = sb("stats", [P, NG, bodies, 6])
        mean_sum = sb("mean_sum", [P, NG])
        dev = sb("dev", [P, NG, means])
        dev2 = sb("dev2", [P, NG, means])
        spread = sb("spread", [P, NG, means])
        spread_sum = sb("spread_sum", [P, NG])
        by_channel = sb("by_channel", [P, 2, NG, CW])
        neg_mean = sb("neg_mean", [P, 1])
        var_eps = sb("var_eps", [P, 1])
        minus_half = sb("minus_half", [P, 1])
        rstd = sb("rstd", [P, 1])
        bias_f = sb("bias_f", [P, K])
        part_hi = sb("part_hi", [P, K], BF16)
        part_mid = sb("part_mid", [P, K], BF16)
        rest = sb("rest", [P, 2, K])

        def banks(name):
            return ctx.enter_context(nc.psum_tensor(name, [P, BANKS, 512], F32))

        xT_ps = banks("xT_ps")
        logit_ps = banks("logit_ps")
        turn_ps = banks("turn_ps")
        mix_ps = banks("mix_ps")

        x_turned = sem("x_turned")
        x_cols = sem("x_cols")
        logits_ready = sem("logits_ready")
        maxed = sem("maxed")
        shifted = sem("shifted")
        logits_turned = sem("logits_turned")
        probs = sem("probs")
        mixed = sem("mixed")
        recips = sem("recips")
        scaled = sem("scaled")
        added = sem("added")
        per_group = [x_turned, x_cols, logits_ready, maxed, shifted, logits_turned,
                     probs, mixed, recips, scaled, added]
        x_loaded = [sem(f"x_loaded{i}") for i in range(XBUFS)]
        out_stored = [sem(f"out_stored{i}") for i in range(OBUFS)]
        slab_loaded = sem("slab_loaded")
        slab_used = sem("slab_used")
        consts_loaded = sem("consts_loaded")
        pool_const = sem("pool_const")
        vec_const = sem("vec_const")
        set_pe = sem("set_pe")
        set_dve = sem("set_dve")
        norm_pe = sem("norm_pe")
        norm_dve = sem("norm_dve")
        norm_pool = sem("norm_pool")
        block = ctx.enter_context(nc.Block())

        def done(g):
            return g + 1 + LEAD

        def body_steps(n, first, stages):
            for k in range(BODY):
                for f, lag in stages:
                    if k >= lag or not first:
                        f(n, n * BODY + (k - lag), (k - lag) % BODY)

        def drain_steps(n, stages):
            for k in range(BODY, BODY + last_lag):
                for f, lag in stages:
                    if k - lag < BODY:
                        f(n, n * BODY + (k - lag), k - lag)

        def tile(ap, buf, t, width=P, step=P):
            return ap[:, buf, t * step:t * step + width]

        NORM_PE, NORM_DVE = 3, 17

        @block.sync
        def _(sp):
            for dst, src in ((Wk_sb[:, :], Wk), (pat_aug[:, 0:C], pattern), (Wq_sb[:, :], Wq),
                             (bq_sb[:, :], bq.rearrange("(p a) -> p a", a=1)),
                             (bk_sb[:, :], bk.rearrange("(p a) -> p a", a=1))):
                sp.dma_start(dst, src).then_inc(consts_loaded, 16)

            def load_slab_piece(q, j):
                sp.dma_start(slab[:, q % 2, j * CHUNK_T * C:(j + 1) * CHUNK_T * C],
                             x_chunks[q * CHUNKS + j]).then_inc(slab_loaded, 16)

            def slab_free(q):
                sp.wait_ge(slab_used, q - 1)
                sp.wait_ge(slab_loaded, 16 * CHUNKS * q)

            def load_x(c, buf):
                sp.dma_start(x_sb[:, buf, :], x_chunks[c]).then_inc(x_loaded[buf], 16)

            for j in range(CHUNKS):
                load_slab_piece(0, j)
            sp.wait_ge(slab_loaded, 16 * CHUNKS)
            for j in range(CHUNKS):
                load_slab_piece(1, j)
            for c in range(XBUFS):
                load_x(c, c)
            with sp.Fori(0, bodies - 1) as i:
                slab_free(i + 2)
                for j in range(CHUNKS):
                    load_slab_piece(i + 2, j)

            def body(n, with_slab, next_x):
                if with_slab:
                    slab_free(n + bodies + 1)
                for m in range(CHUNKS):
                    c = n * CHUNKS + m
                    sp.wait_ge(added, done(n * BODY + m * GROUP_CHUNK + GROUP_CHUNK - 1))
                    sp.dma_start(out_chunks[c], out_sb[:, m % OBUFS, :]).then_inc(out_stored[m % OBUFS], 16)
                    if m < next_x:
                        load_x(c + XBUFS, m % XBUFS)
                    if with_slab:
                        for j in range(m * CHUNKS // SLAB_STEPS, min(CHUNKS, (m + 1) * CHUNKS // SLAB_STEPS)):
                            load_slab_piece(n + bodies + 1, j)

            slab_bodies = all_bodies - bodies - 1
            with sp.Fori(0, slab_bodies) as n:
                body(n, True, CHUNKS)
            with sp.Fori(slab_bodies, all_bodies - 1) as n:
                body(n, False, CHUNKS)
            body(all_bodies - 1, False, CHUNKS - XBUFS)
            for i in range(OBUFS):
                sp.wait_ge(out_stored[i], 16 * (all_bodies * CHUNKS // OBUFS + 1))

        @block.gpsimd
        def _(pool):
            for s in per_group:
                pool.sem_inc(s, LEAD)
            for s in out_stored:
                pool.sem_inc(s, 16)
            pool.memset(ident[:, :], 0.0).then_inc(pool_const, 1)
            pool.memset(mean_w[:, :], 1.0 / (P * means)).then_inc(pool_const, 1)
            pool.memset(ones_bf[:, :], 1.0).then_inc(pool_const, 1)
            pool.memset(minus_half[:, :], -0.5).then_inc(pool_const, 1)
            pool.wait_ge(pool_const, 4)
            pool.affine_select(out=ident[:, :], in_=ident[:, :], compare_op=ALU.not_equal, fill=1.0,
                               base=0, pattern=[[-1, P]], channel_multiplier=1).then_inc(pool_const, 1)

            def body(n):
                for k in range(BODY):
                    m, r = k // GROUP_CHUNK, k % GROUP_CHUNK
                    if r == 0:
                        pool.wait_ge(out_stored[m % OBUFS], (n * (CHUNKS // OBUFS) + (m // OBUFS + 1)) * 16)
                    pool.wait_ge(scaled, done(n * BODY + k))
                    cols = slice(r * TILES * C, (r + 1) * TILES * C)
                    pool.tensor_tensor(out_sb[:, m % OBUFS, cols], x_sb[:, m % XBUFS, cols],
                                       y_sb[:, k % RING, :], ALU.add).then_inc(added, 1)

            with pool.Fori(0, B) as b:
                pool.wait_ge(norm_dve, b * NORM_DVE + 9)
                pool.tensor_tensor(rstd[:, :], var_eps[:, :], minus_half[:, :], ALU.pow).then_inc(norm_pool, 1)
                with pool.Fori(0, bodies) as it:
                    body(b * bodies + it)

        @block.scalar
        def _(act):
            def evacuate_x(n, g, k):
                act.wait_ge(x_turned, done(g))
                act.wait_ge(logits_ready, done(g - RING))
                act.activation(xT_sb[:, k % RING, :], xT_ps[:, k % BANKS, 0:TILES * P],
                               ACT.Copy).then_inc(x_cols, 1)

            def exponential(n, g, k):
                act.wait_ge(logits_turned, done(g))
                act.wait_ge(mixed, done(g - RING))
                act.activation(prob_sb[:, k % RING, :], turn_ps[:, k % BANKS, 0:TILES * P],
                               ACT.Exp).then_inc(probs, 1)

            def scale(n, g, k):
                act.wait_ge(recips, done(g))
                act.wait_ge(added, done(g - RING))
                for t in range(TILES):
                    last = act.activation(tile(y_sb, k % RING, t), tile(mix_ps, k % BANKS, t, C, W1),
                                          ACT.Copy, scale=rsum[:, k % RING, t:t + 1])
                last.then_inc(scaled, 1)

            stages = [(evacuate_x, 0), (scale, 4), (exponential, 2)]
            with act.Fori(0, B) as b:
                body_steps(b * bodies, True, stages)
                with act.Fori(1, bodies) as it:
                    body_steps(b * bodies + it, False, stages)
                drain_steps(b * bodies + (bodies - 1), stages)

        @block.vector
        def _(dve):
            dve.memset(pat_aug[:, C:W1], 1.0).then_inc(vec_const, 1)
            dve.memset(bias_bf[:, :], 0.0).then_inc(vec_const, 1)
            dve.wait_ge(set_pe, 1)
            dve.tensor_copy(WkT_sb[:, :], xT_ps[:, 0, 0:P]).then_inc(set_dve, 1)
            dve.tensor_copy(patT_sb[:, :], xT_ps[:, 0, P:2 * P]).then_inc(set_dve, 1)
            dve.wait_ge(set_pe, 2)
            dve.tensor_scalar(patkT_sb[:, :], logit_ps[:, 0, 0:K], bk_sb[:, 0:1], None, ALU.add).then_inc(set_dve, 1)
            dve.wait_ge(set_pe, 3)
            dve.tensor_scalar(A_sb[:, :], turn_ps[:, 0, 0:K], inv_sqrt_d, None, ALU.mult).then_inc(set_dve, 1)
            dve.tensor_scalar(bias_c[:, :], turn_ps[:, 0, K:2 * K], inv_sqrt_d, None, ALU.mult).then_inc(set_dve, 1)

            def slab_stats(q, it, group):
                view = slab[:, q % 2, :].rearrange("p (t g e) -> p t g e", g=NG, e=CW)
                return dve.bn_stats(stats[:, group, it, :], view[:, :, group, :])

            def normalisation(b):
                step = [0]

                def link(ins):
                    step[0] += 1
                    ins.then_inc(norm_dve, 1)
                    dve.wait_ge(norm_dve, b * NORM_DVE + step[0])

                part = stats[:, :, :, :].rearrange("p g s (h f) -> p g (s h) f", f=3)
                dve.wait_ge(slab_used, (b + 1) * bodies)
                link(dve.tensor_reduce(mean_sum[:, :], part[:, :, :, 1], AX_X, ALU.add))
                dve.wait_ge(norm_pe, b * NORM_PE + 1)
                link(dve.tensor_tensor(dev[:, :, :], part[:, :, :, 1],
                                       logit_ps[:, 0, 0:NG].unsqueeze(2).broadcast_to((P, NG, means)), ALU.subtract))
                link(dve.tensor_tensor(dev2[:, :, :], dev[:, :, :], dev[:, :, :], ALU.mult))
                link(dve.scalar_tensor_tensor(out=spread[:, :, :], in0=part[:, :, :, 2], scalar=1.0 / half_count,
                                              in1=dev2[:, :, :], op0=ALU.mult, op1=ALU.add))
                link(dve.tensor_reduce(spread_sum[:, :], spread[:, :, :], AX_X, ALU.add))
                for i, s in enumerate((mean_sum, spread_sum)):
                    link(dve.tensor_copy(by_channel[:, i], s[:, :].unsqueeze(2).broadcast_to((P, NG, CW))))
                dve.wait_ge(norm_pe, b * NORM_PE + 2)
                link(dve.tensor_scalar(neg_mean[:, :], logit_ps[:, 1, 0:1], -1.0, None, ALU.mult))
                link(dve.tensor_scalar(var_eps[:, :], logit_ps[:, 1, 1:2], EPS, None, ALU.add))
                dve.wait_ge(norm_pool, b + 1)
                link(dve.tensor_scalar(M_sb[:, :], A_sb[:, :], rstd[:, 0:1], None, ALU.mult))
                dve.wait_ge(norm_pe, b * NORM_PE + 3)
                link(dve.tensor_tensor(bias_f[:, :], logit_ps[:, 0, 128:128 + K], bias_c[:, :], ALU.add))
                link(dve.tensor_copy(part_hi[:, :], bias_f[:, :]))
                link(dve.tensor_tensor(rest[:, 0, :], bias_f[:, :], part_hi[:, :], ALU.subtract))
                link(dve.tensor_copy(part_mid[:, :], rest[:, 0, :]))
                link(dve.tensor_tensor(rest[:, 1, :], rest[:, 0, :], part_mid[:, :], ALU.subtract))
                dve.tensor_copy(bias_bf[0:1, :], part_hi[0:1, :])
                link(dve.tensor_copy(bias_bf[32:33, :], part_mid[32:33, :]))
                link(dve.tensor_copy(bias_bf[64:65, :], rest[64:65, 1, :]))
                assert step[0] == NORM_DVE

            def shift(n, g, k):
                dve.wait_ge(logits_ready, done(g))
                logits = logit_ps[:, k % BANKS, 0:TILES * K].rearrange("p (t k) -> p t k", t=TILES)
                dve.tensor_reduce(negmax[:, k % RING, :], logits, AX_X, ALU.max, negate=True).then_inc(maxed, 1)
                dve.wait_ge(maxed, done(g))
                dve.wait_ge(logits_turned, done(g - RING))
                dve.tensor_tensor(shift_sb[:, k % RING, :].rearrange("p (t k) -> p t k", t=TILES), logits,
                                  negmax[:, k % RING, :].unsqueeze(2).broadcast_to((P, TILES, K)),
                                  ALU.add).then_inc(shifted, 1)

            def reciprocal(n, g, k):
                dve.wait_ge(mixed, done(g))
                dve.wait_ge(scaled, done(g - RING))
                sums = mix_ps[:, k % BANKS, 0:TILES * W1].rearrange("p (t c) -> p t c", t=TILES)[:, :, C]
                dve.reciprocal(rsum[:, k % RING, :], sums).then_inc(recips, 1)

            def stages(n, it, with_stats):
                def statistics(_, g, k):
                    if k == 0:
                        dve.wait_ge(slab_loaded, 16 * CHUNKS * (n + bodies + 1))
                    for group in range(k * NG // BODY, (k + 1) * NG // BODY):
                        last = slab_stats(n + bodies, it, group)
                    if k == BODY - 1:
                        last.then_inc(slab_used, 1)

                return [(shift, 0), (reciprocal, 2)] + ([(statistics, 0)] if with_stats else [])

            def batch(b, with_stats):
                n = b * bodies
                normalisation(b)
                body_steps(n, True, stages(n, 0, with_stats))
                with dve.Fori(1, bodies) as it:
                    body_steps(n + it, False, stages(n + it, it, with_stats))
                drain_steps(n + (bodies - 1), [(shift, 0), (reciprocal, 2)])

            with dve.Fori(0, bodies) as q:
                dve.wait_ge(slab_loaded, 16 * CHUNKS * (q + 1))
                for group in range(NG):
                    last = slab_stats(q, q, group)
                last.then_inc(slab_used, 1)
            with dve.Fori(0, B - 1) as b:
                batch(b, True)
            batch(B - 1, False)

        @block.tensor
        def _(pe):
            pe.wait_ge(consts_loaded, 16 * 5)
            pe.wait_ge(pool_const, 5)
            pe.wait_ge(vec_const, 2)
            pe.transpose(xT_ps[:, 0, 0:P], Wk_sb[:, :], ident[:, :])
            pe.transpose(xT_ps[:, 0, P:2 * P], pat_aug[:, 0:C], ident[:, :]).then_inc(set_pe, 1)
            pe.wait_ge(set_dve, 2)
            pe.matmul(logit_ps[:, 0, 0:K], WkT_sb[:, :], patT_sb[:, :], start=True, stop=True).then_inc(set_pe, 1)
            pe.wait_ge(set_dve, 3)
            pe.matmul(turn_ps[:, 0, 0:K], Wq_sb[:, :], patkT_sb[:, :], start=True, stop=True)
            pe.matmul(turn_ps[:, 0, K:2 * K], bq_sb[:, :].broadcast_to((P, P)), patkT_sb[:, :],
                      start=True, stop=True).then_inc(set_pe, 1)
            pe.wait_ge(set_dve, 5)

            def normalisation(b):
                pe.wait_ge(norm_dve, b * NORM_DVE + 1)
                pe.matmul(logit_ps[:, 0, 0:NG], mean_w[:, :], mean_sum[:, :],
                          start=True, stop=True).then_inc(norm_pe, 1)
                pe.wait_ge(norm_dve, b * NORM_DVE + 7)
                for i in range(2):
                    last = pe.matmul(logit_ps[:, 1, i:i + 1], by_channel[:, i].rearrange("p g e -> p (g e)"),
                                     mean_w[:, 0:1], start=True, stop=True)
                last.then_inc(norm_pe, 1)
                pe.wait_ge(norm_dve, b * NORM_DVE + 10)
                pe.matmul(logit_ps[:, 0, 128:128 + K], neg_mean[:, :].broadcast_to((P, P)), M_sb[:, :],
                          start=True, stop=True).then_inc(norm_pe, 1)
                pe.wait_ge(norm_dve, (b + 1) * NORM_DVE)

            def turn_x(n, g, k):
                m, r = k // GROUP_CHUNK, k % GROUP_CHUNK
                if r == 0:
                    pe.wait_ge(x_loaded[m % XBUFS], (n * (CHUNKS // XBUFS) + (m // XBUFS + 1)) * 16)
                pe.wait_ge(x_cols, done(g - BANKS))
                for t in range(TILES):
                    last = pe.transpose(tile(xT_ps, k % BANKS, t), tile(x_sb, m % XBUFS, r * TILES + t), ident[:, :])
                last.then_inc(x_turned, 1)

            def logits(n, g, k):
                pe.wait_ge(x_cols, done(g))
                pe.wait_ge(shifted, done(g - BANKS))
                pe.matmul(logit_ps[:, k % BANKS, 0:TILES * K], ones_bf[:, :],
                          bias_bf[:, :].unsqueeze(1).broadcast_to((P, TILES, K)),
                          start=True, stop=False, skip_group_check=True)
                for t in range(TILES):
                    last = pe.matmul(tile(logit_ps, k % BANKS, t), tile(xT_sb, k % RING, t), M_sb[:, :],
                                     start=False, stop=(t == TILES - 1), skip_group_check=True)
                last.then_inc(logits_ready, 1)

            def turn_logits(n, g, k):
                pe.wait_ge(shifted, done(g))
                pe.wait_ge(probs, done(g - BANKS))
                for t in range(TILES):
                    last = pe.transpose(tile(turn_ps, k % BANKS, t), tile(shift_sb, k % RING, t), ident[:, :])
                last.then_inc(logits_turned, 1)

            def mix(n, g, k):
                pe.wait_ge(probs, done(g))
                pe.wait_ge(scaled, done(g - BANKS))
                for t in range(TILES):
                    last = pe.matmul(tile(mix_ps, k % BANKS, t, W1, W1), tile(prob_sb, k % RING, t), pat_aug[:, :],
                                     start=True, stop=True)
                last.then_inc(mixed, 1)

            stages = [(turn_x, 0), (logits, 1), (turn_logits, 2), (mix, 3)]
            with pe.Fori(0, B) as b:
                normalisation(b)
                body_steps(b * bodies, True, stages)
                with pe.Fori(1, bodies) as it:
                    body_steps(b * bodies + it, False, stages)
                drain_steps(b * bodies + (bodies - 1), stages)


_INS = ['x', 'L0_conv_pattern', 'L0_conv_Wq', 'L0_conv_bq', 'L0_conv_Wk', 'L0_conv_bk']
_OUTS = [((8, 200, 288, 128), 'float32')]


def kernel(**inputs):
    import numpy as _np
    import concourse.bacc as _bacc
    from concourse import mybir as _mybir
    from concourse.bass_utils import run_bass_kernel_spmd as _run

    nc = _bacc.Bacc("TRN2", target_bir_lowering=False, num_devices=1)
    arrays, args = {}, []
    for name in _INS:
        a = _np.ascontiguousarray(inputs[name])
        arrays[f"in_{name}_dram"] = a
        args.append(nc.dram_tensor(f"in_{name}_dram", a.shape, _mybir.dt.from_np(a.dtype), kind="ExternalInput").ap())
    for i, (shape, dtype) in enumerate(_OUTS):
        dt = _mybir.dt.from_np(_np.dtype(dtype))
        args.append(nc.dram_tensor(f"out_{i}_dram", shape, dt, kind="ExternalOutput").ap())
    program(nc, *args)
    r = _run(nc, [arrays], core_ids=[0])
    got = tuple(r.results[0][f"out_{i}_dram"] for i in range(len(_OUTS)))
    return got[0]
```

```python
from contextlib import ExitStack

import concourse.bass as bass
from concourse import mybir

ALU = mybir.AluOpType
ACT = mybir.ActivationFunctionType
F32 = mybir.dt.float32
AX_X = mybir.AxisListType.X

P = 128
TILES = 3
GROUP_CHUNK = 3
CHUNK_T = TILES * GROUP_CHUNK
CHUNKS = 10
BODY = GROUP_CHUNK * CHUNKS
SLAB_CHUNKS = 5
SLAB_T = CHUNK_T * SLAB_CHUNKS
SLAB_BUFS = 5
RESIDENT = 4
RES_CHUNKS = RESIDENT * SLAB_CHUNKS
RES_BODIES = RES_CHUNKS // CHUNKS
NG = 32
EPS = 1e-5
XBUFS = CHUNKS
REFILL_LAG = 9
RING = 3
BANKS = 2
LOWEST = -3.0e38
LEAD = 4


def program(nc, x, pattern, Wq, bq, Wk, bk, out):
    B, H, W_, C = x.shape
    K = pattern.shape[0]
    assert C == P and K == P
    tokens = H * W_
    batch_t = tokens // P
    batch_chunks = batch_t // CHUNK_T
    bodies = batch_chunks // CHUNKS
    slabs = batch_chunks // SLAB_CHUNKS
    assert batch_t == bodies * CHUNKS * CHUNK_T and slabs == 2 * SLAB_BUFS and RES_BODIES * CHUNKS == RES_CHUNKS
    assert tokens == P * batch_t
    all_bodies = B * bodies
    CW = C // NG
    W1 = C + 1
    inv_sqrt_d = float(C) ** -0.5
    half_count = SLAB_T * CW // 2
    means = slabs * 2

    x_chunks = x.rearrange("b h w c -> (b h w c)").rearrange("(n p f) -> n p f", p=P, f=CHUNK_T * C)
    out_chunks = out.rearrange("b h w c -> (b h w c)").rearrange("(n p f) -> n p f", p=P, f=CHUNK_T * C)

    with ExitStack() as ctx:
        def sb(name, shape, dt=F32):
            return ctx.enter_context(nc.sbuf_tensor(name, shape, dt))

        def sem(name):
            return ctx.enter_context(nc.semaphore(name))

        slab = sb("slab", [P, SLAB_BUFS, SLAB_CHUNKS, CHUNK_T * C])
        x_sb = sb("x_sb", [P, XBUFS, CHUNK_T * C])
        xT_sb = sb("xT_sb", [P, RING, TILES * P])
        shift_sb = sb("shift_sb", [P, RING, TILES * K])
        top = sb("top", [P, RING, TILES])
        prob_sb = sb("prob_sb", [P, RING, TILES * P])
        y_sb = sb("y_sb", [P, RING, TILES * C])
        rsum = sb("rsum", [P, RING, TILES])
        ident = sb("ident", [P, P])
        mean_w = sb("mean_w", [P, P])
        pat_aug = sb("pat_aug", [P, W1])
        Wq_sb = sb("Wq_sb", [P, C])
        Wk_sb = sb("Wk_sb", [P, C])
        bq_sb = sb("bq_sb", [P, 1])
        bk_sb = sb("bk_sb", [P, 1])
        WkT_sb = sb("WkT_sb", [P, P])
        patT_sb = sb("patT_sb", [P, P])
        patkT_sb = sb("patkT_sb", [P, K])
        A_sb = sb("A_sb", [P, K])
        bias_c = sb("bias_c", [P, K])
        M_sb = sb("M_sb", [P, K])
        bias_sb = sb("bias_sb", [P, K])
        M_next = sb("M_next", [P, K])
        bias_next = sb("bias_next", [P, K])
        stats = sb("stats", [P, NG, slabs, 6])
        mean_sum = sb("mean_sum", [P, NG])
        dev = sb("dev", [P, NG, means])
        dev2 = sb("dev2", [P, NG, means])
        spread = sb("spread", [P, NG, means])
        spread_sum = sb("spread_sum", [P, NG])
        by_channel = sb("by_channel", [P, 2, NG, CW])
        neg_mean = sb("neg_mean", [P, 1])
        var_eps = sb("var_eps", [P, 1])
        minus_half = sb("minus_half", [P, 1])
        rstd = sb("rstd", [P, 1])

        def banks(name):
            return ctx.enter_context(nc.psum_tensor(name, [P, BANKS, 512], F32))

        xT_ps = banks("xT_ps")
        logit_ps = banks("logit_ps")
        turn_ps = banks("turn_ps")
        mix_ps = banks("mix_ps")

        x_turned = sem("x_turned")
        x_cols = sem("x_cols")
        logits_ready = sem("logits_ready")
        maxed = sem("maxed")
        shifted = sem("shifted")
        logits_turned = sem("logits_turned")
        probs = sem("probs")
        mixed = sem("mixed")
        recips = sem("recips")
        scaled = sem("scaled")
        added = sem("added")
        per_group = [x_turned, x_cols, logits_ready, maxed, shifted, logits_turned,
                     probs, mixed, recips, scaled, added]
        x_loaded = [sem(f"x_loaded{i}") for i in range(XBUFS)]
        out_stored = [sem(f"out_stored{i}") for i in range(2)]
        slab_loaded = [sem(f"slab_loaded{i}") for i in range(SLAB_BUFS)]
        slab_used = sem("slab_used")
        consts_loaded = sem("consts_loaded")
        pool_const = sem("pool_const")
        vec_const = sem("vec_const")
        set_pe = sem("set_pe")
        set_dve = sem("set_dve")
        norm_pe = sem("norm_pe")
        norm_dve = sem("norm_dve")
        norm_pool = sem("norm_pool")
        block = ctx.enter_context(nc.Block())

        def done(g):
            return g + 1 + LEAD

        def work_chunk(a):
            return batch_chunks - RES_CHUNKS + a if a < RES_CHUNKS else a - RES_CHUNKS

        def x_place(a):
            if a < RES_CHUNKS:
                return slab[:, (slabs - RESIDENT + a // SLAB_CHUNKS) % SLAB_BUFS, a % SLAB_CHUNKS, :]
            return x_sb[:, a % XBUFS, :]

        def x_columns(it, k):
            cols = slice(k % GROUP_CHUNK * TILES * C, (k % GROUP_CHUNK + 1) * TILES * C)
            return x_place(first_chunk(it) + k // GROUP_CHUNK)[:, cols]

        def first_chunk(it):
            return it * CHUNKS if isinstance(it, int) and it < RES_BODIES else RES_CHUNKS

        def slab_landed(b, j):
            return (b * (slabs // SLAB_BUFS) + j // SLAB_BUFS + 1) * 16 * SLAB_CHUNKS

        def steps(n, first, count, stages):
            for k in range(first, first + count):
                for f, lag in stages:
                    if k >= lag:
                        f(n, k - lag)

        def drain_steps(n, stages):
            for k in range(BODY, BODY + max(lag for _, lag in stages)):
                for f, lag in stages:
                    if k - lag < BODY:
                        f(n, k - lag)

        def all_batches(eng, fill, unrolled, stages, drain_stages=None):
            def first_bodies(b, unrolled, ahead):
                for it in range(unrolled):
                    steps(b * bodies + it, fill, BODY, stages(b, it, ahead))
                if unrolled < bodies - 1:
                    with eng.Fori(unrolled, bodies - 1) as it:
                        steps(b * bodies + it, fill, BODY, stages(b, it, ahead))

            steps(0, 0, fill, stages(0, 0, False))
            with eng.Fori(0, B - 1) as b:
                first_bodies(b, unrolled, True)
                steps(b * bodies + (bodies - 1), fill, BODY, stages(b, bodies - 1, True))
            first_bodies(B - 1, min(unrolled, RES_BODIES), False)
            last = stages(B - 1, bodies - 1, False)
            steps(all_bodies - 1, fill, BODY - fill, last)
            drain_steps(all_bodies - 1, drain_stages or last)

        def tile(ap, buf, t, width=P, step=P):
            return ap[:, buf, t * step:t * step + width]

        NORM_PE, NORM_DVE = 3, 13
        MEAN_AT, MOMENTS_AT, BIAS_AT = 24, 26, 29
        RSTD_AT = 22
        SPARE = TILES * K

        @block.sync
        def _(sp):
            for dst, src in ((Wk_sb[:, :], Wk), (pat_aug[:, 0:C], pattern), (Wq_sb[:, :], Wq),
                             (bq_sb[:, :], bq.rearrange("(p a) -> p a", a=1)),
                             (bk_sb[:, :], bk.rearrange("(p a) -> p a", a=1))):
                sp.dma_start(dst, src).then_inc(consts_loaded, 16)

            def load_piece(b, j, i):
                sp.dma_start(slab[:, j % SLAB_BUFS, i, :],
                             x_chunks[b * batch_chunks + (j * SLAB_CHUNKS + i)]).then_inc(slab_loaded[j % SLAB_BUFS], 16)

            def load_slab(b, j):
                for i in range(SLAB_CHUNKS):
                    load_piece(b, j, i)

            def load_again(b, i):
                sp.dma_start(x_sb[:, i % XBUFS, :], x_chunks[b * batch_chunks + i]).then_inc(x_loaded[i % XBUFS], 16)

            for j in range(SLAB_BUFS):
                load_slab(0, j)
            for j in range(SLAB_BUFS, slabs):
                sp.wait_ge(slab_used, j - SLAB_BUFS + 1)
                load_slab(0, j)
            for i in range(XBUFS):
                load_again(0, i)
            sp.wait_ge(slab_used, SLAB_BUFS + 1)
            load_slab(1, 0)

            with_work = {2: (1, 5), 3: (1, 6), 4: (1, 7), 5: (1, 8), 6: (1, 9), 7: (2, 0)}

            def wait_stored(b, a):
                sp.wait_ge(out_stored[a % 2], (b * (batch_chunks // 2) + (a // 2 + 1)) * 16)

            def refill(b, a, ahead):
                if a < RES_CHUNKS:
                    if ahead:
                        load_piece(b + 1, 1 + a // SLAB_CHUNKS, a % SLAB_CHUNKS)
                else:
                    nxt = a - RES_CHUNKS + XBUFS
                    if nxt < batch_chunks - RES_CHUNKS:
                        load_again(b, nxt)
                    elif ahead:
                        load_again(b + 1, nxt - (batch_chunks - RES_CHUNKS))

            def batch(b, ahead):
                for a in range(batch_chunks):
                    sp.wait_ge(added, done(b * (bodies * BODY) + (a * GROUP_CHUNK + GROUP_CHUNK - 1)))
                    sp.dma_start(out_chunks[b * batch_chunks + work_chunk(a)],
                                 x_place(a)).then_inc(out_stored[a % 2], 16)
                    step, j = with_work.get(a // SLAB_CHUNKS, (B, 0))
                    if step <= ahead:
                        if a % SLAB_CHUNKS == 0:
                            sp.wait_ge(slab_used, (b + step) * slabs + (j - SLAB_BUFS + 1))
                        load_piece(b + step, j, a % SLAB_CHUNKS)
                    if a > 0:
                        wait_stored(b, a - 1)
                        refill(b, a - 1, ahead)
                wait_stored(b, batch_chunks - 1)
                refill(b, batch_chunks - 1, ahead)

            with sp.Fori(0, B - 2) as b:
                batch(b, 2)
            batch(B - 2, 1)
            batch(B - 1, 0)

        @block.gpsimd
        def _(pool):
            for s in per_group:
                pool.sem_inc(s, LEAD)
            pool.memset(ident[:, :], 0.0).then_inc(pool_const, 1)
            pool.memset(mean_w[:, :], 1.0 / (P * means)).then_inc(pool_const, 1)
            pool.memset(minus_half[:, :], -0.5).then_inc(pool_const, 1)
            pool.wait_ge(pool_const, 3)
            pool.affine_select(out=ident[:, :], in_=ident[:, :], compare_op=ALU.not_equal, fill=1.0,
                               base=0, pattern=[[-1, P]], channel_multiplier=1).then_inc(pool_const, 1)

            def inverse_std(b):
                pool.wait_ge(norm_dve, b * NORM_DVE + 9)
                pool.tensor_tensor(rstd[:, :], var_eps[:, :], minus_half[:, :], ALU.pow).then_inc(norm_pool, 1)

            def body(b, it, ahead):
                n = b * bodies + it
                for k in range(BODY):
                    if ahead and k == RSTD_AT:
                        inverse_std(b + 1)
                    pool.wait_ge(scaled, done(n * BODY + k))
                    pool.tensor_tensor(x_columns(it, k), x_columns(it, k), y_sb[:, k % RING, :],
                                       ALU.add).then_inc(added, 1)

            def batch(b, ahead):
                for it in range(RES_BODIES):
                    body(b, it, False)
                with pool.Fori(RES_BODIES, bodies - 1) as it:
                    body(b, it, False)
                body(b, bodies - 1, ahead)

            inverse_std(0)
            with pool.Fori(0, B - 1) as b:
                batch(b, True)
            batch(B - 1, False)

        @block.scalar
        def _(act):
            def evacuate_x(n, k):
                g = n * BODY + k
                act.wait_ge(x_turned, done(g))
                act.wait_ge(logits_ready, done(g - RING))
                act.activation(xT_sb[:, k % RING, :], xT_ps[:, k % BANKS, 0:TILES * P],
                               ACT.Copy).then_inc(x_cols, 1)

            def exponential(n, k):
                g = n * BODY + k
                act.wait_ge(logits_turned, done(g))
                act.wait_ge(mixed, done(g - RING))
                act.activation(prob_sb[:, k % RING, :], turn_ps[:, k % BANKS, 0:TILES * P],
                               ACT.Exp).then_inc(probs, 1)

            def scale(n, k):
                g = n * BODY + k
                act.wait_ge(recips, done(g))
                act.wait_ge(added, done(g - RING))
                for t in range(TILES):
                    last = act.activation(tile(y_sb, k % RING, t), tile(mix_ps, k % BANKS, t, C, W1),
                                          ACT.Copy, scale=rsum[:, k % RING, t:t + 1])
                last.then_inc(scaled, 1)

            stages = [(evacuate_x, 0), (scale, 4), (exponential, 2)]
            all_batches(act, 4, 0, lambda b, it, ahead: stages)

        @block.vector
        def _(dve):
            dve.memset(pat_aug[:, C:W1], 1.0).then_inc(vec_const, 1)
            dve.wait_ge(set_pe, 1)
            dve.tensor_copy(WkT_sb[:, :], xT_ps[:, 0, 0:P]).then_inc(set_dve, 1)
            dve.tensor_copy(patT_sb[:, :], xT_ps[:, 0, P:2 * P]).then_inc(set_dve, 1)
            dve.wait_ge(set_pe, 2)
            dve.tensor_scalar(patkT_sb[:, :], logit_ps[:, 0, 0:K], bk_sb[:, 0:1], None, ALU.add).then_inc(set_dve, 1)
            dve.wait_ge(set_pe, 3)
            dve.tensor_scalar(A_sb[:, :], turn_ps[:, 0, 0:K], inv_sqrt_d, None, ALU.mult).then_inc(set_dve, 1)
            dve.tensor_scalar(bias_c[:, :], turn_ps[:, 0, K:2 * K], inv_sqrt_d, None, ALU.mult).then_inc(set_dve, 1)

            def slab_stats(buf, j, group):
                view = slab[:, buf].rearrange("p i (t g e) -> p (i t) g e", g=NG, e=CW)
                return dve.bn_stats(stats[:, group, j, :], view[:, :, group, :])

            RECIP_LAG = 3

            def normalisation(b):
                step = [0]

                def link(ins):
                    step[0] += 1
                    ins.then_inc(norm_dve, 1)
                    dve.wait_ge(norm_dve, b * NORM_DVE + step[0])

                def by_channels(i, s):
                    link(dve.tensor_copy(by_channel[:, i], s[:, :].unsqueeze(2).broadcast_to((P, NG, CW))))

                part = stats[:, :, :, :].rearrange("p g s (h f) -> p g (s h) f", f=3)

                def sum_of_means():
                    dve.wait_ge(slab_used, (b + 1) * slabs)
                    link(dve.tensor_reduce(mean_sum[:, :], part[:, :, :, 1], AX_X, ALU.add))
                    by_channels(0, mean_sum)

                def deviations():
                    dve.wait_ge(norm_pe, b * NORM_PE + 1)
                    mean = logit_ps[:, MEAN_AT % BANKS, SPARE:SPARE + NG].unsqueeze(2).broadcast_to((P, NG, means))
                    link(dve.tensor_tensor(dev[:, :, :], part[:, :, :, 1], mean, ALU.subtract))

                def squares():
                    link(dve.tensor_tensor(dev2[:, :, :], dev[:, :, :], dev[:, :, :], ALU.mult))
                    link(dve.scalar_tensor_tensor(out=spread[:, :, :], in0=part[:, :, :, 2],
                                                  scalar=1.0 / half_count, in1=dev2[:, :, :],
                                                  op0=ALU.mult, op1=ALU.add))

                def sum_of_squares():
                    link(dve.tensor_reduce(spread_sum[:, :], spread[:, :, :], AX_X, ALU.add))
                    by_channels(1, spread_sum)

                def moments():
                    dve.wait_ge(norm_pe, b * NORM_PE + 2)
                    got = logit_ps[:, MOMENTS_AT % BANKS, SPARE:SPARE + 2]
                    link(dve.tensor_scalar(neg_mean[:, :], got[:, 0:1], -1.0, None, ALU.mult))
                    link(dve.tensor_scalar(var_eps[:, :], got[:, 1:2], EPS, None, ALU.add))

                def scale_rows():
                    dve.wait_ge(norm_pool, b + 1)
                    link(dve.tensor_scalar(M_next[:, :], A_sb[:, :], rstd[:, 0:1], None, ALU.mult))

                def bias():
                    dve.wait_ge(norm_pe, b * NORM_PE + 3)
                    link(dve.tensor_tensor(bias_next[:, :], logit_ps[:, BIAS_AT % BANKS, SPARE:SPARE + K],
                                           bias_c[:, :], ALU.add))

                def switch():
                    link(dve.tensor_copy(M_sb[:, :], M_next[:, :]))

                return {MEAN_AT - 1: [sum_of_means], MEAN_AT: [deviations, squares],
                        MOMENTS_AT - 1: [sum_of_squares], MOMENTS_AT: [moments], BIAS_AT - 1: [scale_rows],
                        BIAS_AT: [bias, switch]}

            def switch_bias(b):
                dve.tensor_copy(bias_sb[:, :], bias_next[:, :]).then_inc(norm_dve, 1)
                dve.wait_ge(norm_dve, (b + 1) * NORM_DVE)

            def shift(n, k, between=()):
                g = n * BODY + k
                dve.wait_ge(logits_ready, done(g))
                for f in between:
                    f()
                if k >= RECIP_LAG:
                    reciprocal(n, k - RECIP_LAG)
                for t in range(TILES):
                    own = tile(logit_ps, k % BANKS, t)
                    last = dve.tensor_tensor_reduce(own, own, bias_sb[:, :], 1.0, LOWEST, ALU.add, ALU.max,
                                                    top[:, k % RING, t:t + 1])
                last.then_inc(maxed, 1)
                dve.wait_ge(maxed, done(g))
                dve.wait_ge(logits_turned, done(g - RING))
                dve.tensor_tensor(shift_sb[:, k % RING, :].rearrange("p (t k) -> p t k", t=TILES),
                                  logit_ps[:, k % BANKS, 0:TILES * K].rearrange("p (t k) -> p t k", t=TILES),
                                  top[:, k % RING, :].unsqueeze(2).broadcast_to((P, TILES, K)),
                                  ALU.subtract).then_inc(shifted, 1)

            def reciprocal(n, k):
                g = n * BODY + k
                dve.wait_ge(mixed, done(g))
                dve.wait_ge(scaled, done(g - RING))
                sums = mix_ps[:, k % BANKS, 0:TILES * W1].rearrange("p (t c) -> p t c", t=TILES)[:, :, C]
                dve.reciprocal(rsum[:, k % RING, :], sums).then_inc(recips, 1)

            stats_at = [0] + [j * GROUP_CHUNK * SLAB_CHUNKS + REFILL_LAG for j in range(1, RESIDENT)]
            even_from = RESIDENT * GROUP_CHUNK * SLAB_CHUNKS + REFILL_LAG
            stats_end = (bodies - 1) * BODY + MEAN_AT - 1 - RECIP_LAG
            stats_at += [even_from + (stats_end - even_from) * i // (slabs - RESIDENT)
                         for i in range(slabs - RESIDENT + 1)]

            def stages(b, it, ahead):
                norm = normalisation(b + 1) if ahead and it == bodies - 1 else {}

                def statistics(_, k):
                    at = it * BODY + (k - RECIP_LAG)
                    if at >= stats_end:
                        return
                    j = max(i for i in range(slabs) if stats_at[i] <= at)
                    begin, span = stats_at[j], stats_at[j + 1] - stats_at[j]
                    if at == begin:
                        dve.wait_ge(slab_loaded[j % SLAB_BUFS], slab_landed(b + 1, j))
                    for group in range((at - begin) * NG // span, (at - begin + 1) * NG // span):
                        last = slab_stats(j % SLAB_BUFS, j, group)
                        if group == NG - 1:
                            last.then_inc(slab_used, 1)

                def shift_and_norm(n, k):
                    if norm and k == BODY:
                        switch_bias(b + 1)
                    shift(n, k, norm.get(k, ()))

                return [(shift_and_norm, 0)] + ([(statistics, 0)] if ahead else [])

            with dve.Fori(0, slabs // SLAB_BUFS) as h:
                for buf in range(SLAB_BUFS):
                    dve.wait_ge(slab_loaded[buf], 16 * SLAB_CHUNKS * (h + 1))
                    for group in range(NG):
                        last = slab_stats(buf, h * SLAB_BUFS + buf, group)
                    last.then_inc(slab_used, 1)
            for fs in normalisation(0).values():
                for f in fs:
                    f()
            switch_bias(0)
            all_batches(dve, RECIP_LAG, bodies - 1, stages, [(reciprocal, RECIP_LAG)])

        @block.tensor
        def _(pe):
            pe.wait_ge(consts_loaded, 16 * 5)
            pe.wait_ge(pool_const, 4)
            pe.wait_ge(vec_const, 1)
            pe.transpose(xT_ps[:, 0, 0:P], Wk_sb[:, :], ident[:, :])
            pe.transpose(xT_ps[:, 0, P:2 * P], pat_aug[:, 0:C], ident[:, :]).then_inc(set_pe, 1)
            pe.wait_ge(set_dve, 2)
            pe.matmul(logit_ps[:, 0, 0:K], WkT_sb[:, :], patT_sb[:, :], start=True, stop=True).then_inc(set_pe, 1)
            pe.wait_ge(set_dve, 3)
            pe.matmul(turn_ps[:, 0, 0:K], Wq_sb[:, :], patkT_sb[:, :], start=True, stop=True)
            pe.matmul(turn_ps[:, 0, K:2 * K], bq_sb[:, :].broadcast_to((P, P)), patkT_sb[:, :],
                      start=True, stop=True).then_inc(set_pe, 1)
            pe.wait_ge(set_dve, 5)

            def norm_product(b, k):
                if k == MEAN_AT:
                    pe.wait_ge(norm_dve, b * NORM_DVE + 1)
                    pe.matmul(logit_ps[:, k % BANKS, SPARE:SPARE + NG], mean_w[:, :], mean_sum[:, :],
                              start=True, stop=True).then_inc(norm_pe, 1)
                if k == MOMENTS_AT:
                    pe.wait_ge(norm_dve, b * NORM_DVE + 7)
                    for i in range(2):
                        last = pe.matmul(logit_ps[:, k % BANKS, SPARE + i:SPARE + i + 1],
                                         by_channel[:, i].rearrange("p g e -> p (g e)"),
                                         mean_w[:, 0:1], start=True, stop=True)
                    last.then_inc(norm_pe, 1)
                if k == BIAS_AT:
                    pe.wait_ge(norm_dve, b * NORM_DVE + 10)
                    pe.matmul(logit_ps[:, k % BANKS, SPARE:SPARE + K], neg_mean[:, :].broadcast_to((P, P)),
                              M_next[:, :], start=True, stop=True).then_inc(norm_pe, 1)
                if k == BODY:
                    pe.wait_ge(norm_dve, b * NORM_DVE + 12)

            def turn_x(n, k, b, it):
                if k >= BODY:
                    k_next, k = k, k - BODY
                    b, it = (b + 1, 0) if isinstance(it, int) and it == bodies - 1 else (b, it + 1)
                    g = n * BODY + k_next
                else:
                    g = n * BODY + k
                if first_chunk(it) == RES_CHUNKS and k % GROUP_CHUNK == 0:
                    pe.wait_ge(x_loaded[k // GROUP_CHUNK], (b * (bodies - RES_BODIES) + (it - (RES_BODIES - 1))) * 16)
                pe.wait_ge(x_cols, done(g - BANKS))
                x_now = x_columns(it, k)
                for t in range(TILES):
                    last = pe.transpose(tile(xT_ps, k % BANKS, t), x_now[:, t * C:(t + 1) * C], ident[:, :])
                last.then_inc(x_turned, 1)

            def logits(n, k, next_batch=None):
                g = n * BODY + k
                pe.wait_ge(x_cols, done(g))
                pe.wait_ge(shifted, done(g - BANKS))
                if next_batch is not None:
                    norm_product(next_batch, k)
                for t in range(TILES):
                    last = pe.matmul(tile(logit_ps, k % BANKS, t), tile(xT_sb, k % RING, t), M_sb[:, :],
                                     start=True, stop=True)
                last.then_inc(logits_ready, 1)

            def turn_logits(n, k):
                g = n * BODY + k
                pe.wait_ge(shifted, done(g))
                pe.wait_ge(probs, done(g - BANKS))
                for t in range(TILES):
                    last = pe.transpose(tile(turn_ps, k % BANKS, t), tile(shift_sb, k % RING, t), ident[:, :])
                last.then_inc(logits_turned, 1)

            def mix(n, k):
                g = n * BODY + k
                pe.wait_ge(probs, done(g))
                pe.wait_ge(scaled, done(g - BANKS))
                for t in range(TILES):
                    last = pe.matmul(tile(mix_ps, k % BANKS, t, W1, W1), tile(prob_sb, k % RING, t), pat_aug[:, :],
                                     start=True, stop=True)
                last.then_inc(mixed, 1)

            def stages(b, it, ahead):
                carried = b + 1 if ahead and isinstance(it, int) and it == bodies - 1 else None
                return [(lambda n, k: turn_x(n, k, b, it), 0), (lambda n, k: logits(n, k, carried), 1),
                        (turn_logits, 2), (mix, 3)]

            for k in (MEAN_AT, MOMENTS_AT, BIAS_AT, BODY):
                norm_product(0, k)
            all_batches(pe, 3, RES_BODIES, stages)


_INS = ['x', 'L0_conv_pattern', 'L0_conv_Wq', 'L0_conv_bq', 'L0_conv_Wk', 'L0_conv_bk']
_OUTS = [((8, 200, 288, 128), 'float32')]


def kernel(**inputs):
    import numpy as _np
    import concourse.bacc as _bacc
    from concourse import mybir as _mybir
    from concourse.bass_utils import run_bass_kernel_spmd as _run

    nc = _bacc.Bacc("TRN2", target_bir_lowering=False, num_devices=1)
    arrays, args = {}, []
    for name in _INS:
        a = _np.ascontiguousarray(inputs[name])
        arrays[f"in_{name}_dram"] = a
        args.append(nc.dram_tensor(f"in_{name}_dram", a.shape, _mybir.dt.from_np(a.dtype), kind="ExternalInput").ap())
    for i, (shape, dtype) in enumerate(_OUTS):
        dt = _mybir.dt.from_np(_np.dtype(dtype))
        args.append(nc.dram_tensor(f"out_{i}_dram", shape, dt, kind="ExternalOutput").ap())
    program(nc, *args)
    r = _run(nc, [arrays], core_ids=[0])
    got = tuple(r.results[0][f"out_{i}_dram"] for i in range(len(_OUTS)))
    return got[0]
```

```python
from contextlib import ExitStack

import concourse.bass as bass
from concourse import mybir

ALU = mybir.AluOpType
ACT = mybir.ActivationFunctionType
F32 = mybir.dt.float32
AX_X = mybir.AxisListType.X

P = 128
TILES = 3
GROUP_CHUNK = 3
CHUNK_T = TILES * GROUP_CHUNK
CHUNKS = 10
BODY = GROUP_CHUNK * CHUNKS
SLAB_CHUNKS = 5
SLAB_T = CHUNK_T * SLAB_CHUNKS
SLAB_BUFS = 5
RESIDENT = 4
RES_CHUNKS = RESIDENT * SLAB_CHUNKS
RES_BODIES = RES_CHUNKS // CHUNKS
NG = 32
EPS = 1e-5
XBUFS = CHUNKS
REFILL_LAG = 9
RING = 3
BANKS = 2
LOWEST = -3.0e38
LEAD = 4


def program(nc, x, pattern, Wq, bq, Wk, bk, out):
    B, H, W_, C = x.shape
    K = pattern.shape[0]
    assert C == P and K == P
    tokens = H * W_
    batch_t = tokens // P
    batch_chunks = batch_t // CHUNK_T
    bodies = batch_chunks // CHUNKS
    slabs = batch_chunks // SLAB_CHUNKS
    assert batch_t == bodies * CHUNKS * CHUNK_T and slabs == 2 * SLAB_BUFS and RES_BODIES * CHUNKS == RES_CHUNKS
    assert tokens == P * batch_t
    all_bodies = B * bodies
    CW = C // NG
    W1 = C + 1
    inv_sqrt_d = float(C) ** -0.5
    half_count = SLAB_T * CW // 2
    means = slabs * 2

    x_chunks = x.rearrange("b h w c -> (b h w c)").rearrange("(n p f) -> n p f", p=P, f=CHUNK_T * C)
    out_chunks = out.rearrange("b h w c -> (b h w c)").rearrange("(n p f) -> n p f", p=P, f=CHUNK_T * C)

    with ExitStack() as ctx:
        def sb(name, shape, dt=F32):
            return ctx.enter_context(nc.sbuf_tensor(name, shape, dt))

        def sem(name):
            return ctx.enter_context(nc.semaphore(name))

        slab = sb("slab", [P, SLAB_BUFS, SLAB_CHUNKS, CHUNK_T * C])
        x_sb = sb("x_sb", [P, XBUFS, CHUNK_T * C])
        xT_sb = sb("xT_sb", [P, RING, TILES * P])
        shift_sb = sb("shift_sb", [P, RING, TILES * K])
        top = sb("top", [P, RING, TILES])
        prob_sb = sb("prob_sb", [P, RING, TILES * P])
        y_sb = sb("y_sb", [P, RING, TILES * C])
        rsum = sb("rsum", [P, RING, TILES])
        ident = sb("ident", [P, P])
        mean_w = sb("mean_w", [P, P])
        pat_aug = sb("pat_aug", [P, W1])
        Wq_sb = sb("Wq_sb", [P, C])
        Wk_sb = sb("Wk_sb", [P, C])
        bq_sb = sb("bq_sb", [P, 1])
        bk_sb = sb("bk_sb", [P, 1])
        WkT_sb = sb("WkT_sb", [P, P])
        patT_sb = sb("patT_sb", [P, P])
        patkT_sb = sb("patkT_sb", [P, K])
        A_sb = sb("A_sb", [P, K])
        bias_c = sb("bias_c", [P, K])
        M_sb = sb("M_sb", [P, 2, K])
        bias_sb = sb("bias_sb", [P, K])
        stats = sb("stats", [P, NG, slabs, 6])
        mean_sum = sb("mean_sum", [P, NG])
        dev = sb("dev", [P, NG, means])
        dev2 = sb("dev2", [P, NG, means])
        spread = sb("spread", [P, NG, means])
        spread_sum = sb("spread_sum", [P, NG])
        by_channel = sb("by_channel", [P, 2, NG, CW])
        neg_mean = sb("neg_mean", [P, 1])
        var_eps = sb("var_eps", [P, 1])
        minus_half = sb("minus_half", [P, 1])
        part_weight = sb("part_weight", [P, NG])
        rstd = sb("rstd", [P, 1])

        def banks(name):
            return ctx.enter_context(nc.psum_tensor(name, [P, BANKS, 512], F32))

        xT_ps = banks("xT_ps")
        logit_ps = banks("logit_ps")
        turn_ps = banks("turn_ps")
        mix_ps = banks("mix_ps")

        x_turned = sem("x_turned")
        x_cols = sem("x_cols")
        logits_ready = sem("logits_ready")
        maxed = sem("maxed")
        shifted = sem("shifted")
        logits_turned = sem("logits_turned")
        probs = sem("probs")
        mixed = sem("mixed")
        recips = sem("recips")
        scaled = sem("scaled")
        added = sem("added")
        per_group = [x_turned, x_cols, logits_ready, maxed, shifted, logits_turned,
                     probs, mixed, recips, scaled, added]
        x_loaded = [sem(f"x_loaded{i}") for i in range(XBUFS)]
        out_stored = [sem(f"out_stored{i}") for i in range(2)]
        slab_loaded = [sem(f"slab_loaded{i}") for i in range(SLAB_BUFS)]
        slab_used = sem("slab_used")
        consts_loaded = sem("consts_loaded")
        pool_const = sem("pool_const")
        vec_const = sem("vec_const")
        set_pe = sem("set_pe")
        set_dve = sem("set_dve")
        norm_pe = sem("norm_pe")
        norm_dve = sem("norm_dve")
        norm_pool = sem("norm_pool")
        block = ctx.enter_context(nc.Block())

        def done(g):
            return g + 1 + LEAD

        def work_chunk(a):
            return batch_chunks - RES_CHUNKS + a if a < RES_CHUNKS else a - RES_CHUNKS

        def x_place(a):
            if a < RES_CHUNKS:
                return slab[:, (slabs - RESIDENT + a // SLAB_CHUNKS) % SLAB_BUFS, a % SLAB_CHUNKS, :]
            return x_sb[:, a % XBUFS, :]

        def x_columns(it, k):
            cols = slice(k % GROUP_CHUNK * TILES * C, (k % GROUP_CHUNK + 1) * TILES * C)
            return x_place(first_chunk(it) + k // GROUP_CHUNK)[:, cols]

        def first_chunk(it):
            return it * CHUNKS if isinstance(it, int) and it < RES_BODIES else RES_CHUNKS

        def batch_at(b, it, k):
            return b + 1 if k >= BODY and isinstance(it, int) and it == bodies - 1 else b

        def slab_landed(b, j):
            return (b * (slabs // SLAB_BUFS) + j // SLAB_BUFS + 1) * 16 * SLAB_CHUNKS

        def steps(n, first, count, stages):
            for k in range(first, first + count):
                for f, lag in stages:
                    if k >= lag:
                        f(n, k - lag)

        def drain_steps(n, stages):
            for k in range(BODY, BODY + max(lag for _, lag in stages)):
                for f, lag in stages:
                    if k - lag < BODY:
                        f(n, k - lag)

        def all_batches(eng, fill, unrolled, stages, drain_stages=None):
            def first_bodies(b, unrolled, ahead):
                for it in range(unrolled):
                    steps(b * bodies + it, fill, BODY, stages(b, it, ahead))
                if unrolled < bodies - 1:
                    with eng.Fori(unrolled, bodies - 1) as it:
                        steps(b * bodies + it, fill, BODY, stages(b, it, ahead))

            steps(0, 0, fill, stages(0, 0, False))
            with eng.Fori(0, B - 1) as b:
                first_bodies(b, unrolled, True)
                steps(b * bodies + (bodies - 1), fill, BODY, stages(b, bodies - 1, True))
            first_bodies(B - 1, min(unrolled, RES_BODIES), False)
            last = stages(B - 1, bodies - 1, False)
            steps(all_bodies - 1, fill, BODY - fill, last)
            drain_steps(all_bodies - 1, drain_stages or last)

        def tile(ap, buf, t, width=P, step=P):
            return ap[:, buf, t * step:t * step + width]

        NORM_PE, NORM_DVE, NORM_POOL = 3, 9, 4
        MEAN_AT, MOMENTS_AT, BIAS_AT = 23, 27, BODY
        SPARE = TILES * K

        @block.sync
        def _(sp):
            for dst, src in ((Wk_sb[:, :], Wk), (pat_aug[:, 0:C], pattern), (Wq_sb[:, :], Wq),
                             (bq_sb[:, :], bq.rearrange("(p a) -> p a", a=1)),
                             (bk_sb[:, :], bk.rearrange("(p a) -> p a", a=1))):
                sp.dma_start(dst, src).then_inc(consts_loaded, 16)

            def load_piece(b, j, i):
                sp.dma_start(slab[:, j % SLAB_BUFS, i, :],
                             x_chunks[b * batch_chunks + (j * SLAB_CHUNKS + i)]).then_inc(slab_loaded[j % SLAB_BUFS], 16)

            def load_slab(b, j):
                for i in range(SLAB_CHUNKS):
                    load_piece(b, j, i)

            def load_again(b, i):
                sp.dma_start(x_sb[:, i % XBUFS, :], x_chunks[b * batch_chunks + i]).then_inc(x_loaded[i % XBUFS], 16)

            for j in range(SLAB_BUFS):
                load_slab(0, j)
            for j in range(SLAB_BUFS, slabs):
                sp.wait_ge(slab_used, j - SLAB_BUFS + 1)
                load_slab(0, j)
            for i in range(XBUFS):
                load_again(0, i)
            sp.wait_ge(slab_used, SLAB_BUFS + 1)
            load_slab(1, 0)

            with_work = {2: (1, 5), 3: (1, 6), 4: (1, 7), 5: (1, 8), 6: (1, 9), 7: (2, 0)}

            def wait_stored(b, a):
                sp.wait_ge(out_stored[a % 2], (b * (batch_chunks // 2) + (a // 2 + 1)) * 16)

            def refill(b, a, ahead):
                if a < RES_CHUNKS:
                    if ahead:
                        load_piece(b + 1, 1 + a // SLAB_CHUNKS, a % SLAB_CHUNKS)
                else:
                    nxt = a - RES_CHUNKS + XBUFS
                    if nxt < batch_chunks - RES_CHUNKS:
                        load_again(b, nxt)
                    elif ahead:
                        load_again(b + 1, nxt - (batch_chunks - RES_CHUNKS))

            def batch(b, ahead):
                for a in range(batch_chunks):
                    sp.wait_ge(added, done(b * (bodies * BODY) + (a * GROUP_CHUNK + GROUP_CHUNK - 1)))
                    sp.dma_start(out_chunks[b * batch_chunks + work_chunk(a)],
                                 x_place(a)).then_inc(out_stored[a % 2], 16)
                    step, j = with_work.get(a // SLAB_CHUNKS, (B, 0))
                    if step <= ahead:
                        if a % SLAB_CHUNKS == 0:
                            sp.wait_ge(slab_used, (b + step) * slabs + (j - SLAB_BUFS + 1))
                        load_piece(b + step, j, a % SLAB_CHUNKS)
                    if a > 0:
                        wait_stored(b, a - 1)
                        refill(b, a - 1, ahead)
                wait_stored(b, batch_chunks - 1)
                refill(b, batch_chunks - 1, ahead)

            with sp.Fori(0, B - 2) as b:
                batch(b, 2)
            batch(B - 2, 1)
            batch(B - 1, 0)

        @block.gpsimd
        def _(pool):
            for s in per_group:
                pool.sem_inc(s, LEAD)
            pool.memset(part_weight[:, :], 1.0 / half_count).then_inc(pool_const, 1)
            pool.memset(ident[:, :], 0.0).then_inc(pool_const, 1)
            pool.memset(mean_w[:, :], 1.0 / (P * means)).then_inc(pool_const, 1)
            pool.memset(minus_half[:, :], -0.5).then_inc(pool_const, 1)
            pool.wait_ge(pool_const, 4)
            pool.affine_select(out=ident[:, :], in_=ident[:, :], compare_op=ALU.not_equal, fill=1.0,
                               base=0, pattern=[[-1, P]], channel_multiplier=1).then_inc(pool_const, 1)

            def own_variances(b):
                pool.wait_ge(norm_dve, b * NORM_DVE + 1)
                own = stats[:, :, :, :].rearrange("p g s (h f) -> p g (s h) f", f=3)[:, :, :, 2]
                weight = part_weight[:, :].unsqueeze(2).broadcast_to((P, NG, means))
                pool.tensor_tensor(spread[:, :, :], own, weight, ALU.mult).then_inc(norm_pool, 1)

            def squares(b):
                pool.wait_ge(norm_dve, b * NORM_DVE + 3)
                pool.tensor_tensor(dev2[:, :, :], dev[:, :, :], dev[:, :, :], ALU.mult).then_inc(norm_pool, 1)

            def both(b):
                pool.wait_ge(norm_pool, b * NORM_POOL + 2)
                pool.tensor_tensor(spread[:, :, :], spread[:, :, :], dev2[:, :, :], ALU.add).then_inc(norm_pool, 1)

            def inverse_std(b):
                pool.wait_ge(norm_dve, b * NORM_DVE + 7)
                pool.tensor_tensor(rstd[:, :], var_eps[:, :], minus_half[:, :], ALU.pow).then_inc(norm_pool, 1)

            norm = {MEAN_AT - 4: [own_variances], MEAN_AT - 3: [squares, both], MOMENTS_AT - 3: [inverse_std]}

            def body(b, it, ahead):
                n = b * bodies + it
                for k in range(BODY):
                    for f in norm.get(k, ()) if ahead else ():
                        f(b + 1)
                    pool.wait_ge(scaled, done(n * BODY + k))
                    pool.tensor_tensor(x_columns(it, k), x_columns(it, k), y_sb[:, k % RING, :],
                                       ALU.add).then_inc(added, 1)

            def batch(b, ahead):
                for it in range(RES_BODIES):
                    body(b, it, False)
                with pool.Fori(RES_BODIES, bodies - 1) as it:
                    body(b, it, False)
                body(b, bodies - 1, ahead)

            for fs in norm.values():
                for f in fs:
                    f(0)
            with pool.Fori(0, B - 1) as b:
                batch(b, True)
            batch(B - 1, False)

        @block.scalar
        def _(act):
            def evacuate_x(n, k):
                g = n * BODY + k
                act.wait_ge(x_turned, done(g))
                act.wait_ge(logits_ready, done(g - RING))
                act.activation(xT_sb[:, k % RING, :], xT_ps[:, k % BANKS, 0:TILES * P],
                               ACT.Copy).then_inc(x_cols, 1)

            def exponential(n, k):
                g = n * BODY + k
                act.wait_ge(logits_turned, done(g))
                act.wait_ge(mixed, done(g - RING))
                act.activation(prob_sb[:, k % RING, :], turn_ps[:, k % BANKS, 0:TILES * P],
                               ACT.Exp).then_inc(probs, 1)

            def scale(n, k):
                g = n * BODY + k
                act.wait_ge(recips, done(g))
                act.wait_ge(added, done(g - RING))
                for t in range(TILES):
                    last = act.activation(tile(y_sb, k % RING, t), tile(mix_ps, k % BANKS, t, C, W1),
                                          ACT.Copy, scale=rsum[:, k % RING, t:t + 1])
                last.then_inc(scaled, 1)

            stages = [(evacuate_x, 0), (scale, 4), (exponential, 2)]
            all_batches(act, 4, 0, lambda b, it, ahead: stages)

        @block.vector
        def _(dve):
            dve.memset(pat_aug[:, C:W1], 1.0).then_inc(vec_const, 1)
            dve.wait_ge(set_pe, 1)
            dve.tensor_copy(WkT_sb[:, :], xT_ps[:, 0, 0:P]).then_inc(set_dve, 1)
            dve.tensor_copy(patT_sb[:, :], xT_ps[:, 0, P:2 * P]).then_inc(set_dve, 1)
            dve.wait_ge(set_pe, 2)
            dve.tensor_scalar(patkT_sb[:, :], logit_ps[:, 0, 0:K], bk_sb[:, 0:1], None, ALU.add).then_inc(set_dve, 1)
            dve.wait_ge(set_pe, 3)
            dve.tensor_scalar(A_sb[:, :], turn_ps[:, 0, 0:K], inv_sqrt_d, None, ALU.mult).then_inc(set_dve, 1)
            dve.tensor_scalar(bias_c[:, :], turn_ps[:, 0, K:2 * K], inv_sqrt_d, None, ALU.mult).then_inc(set_dve, 1)

            def slab_stats(buf, j, group):
                view = slab[:, buf].rearrange("p i (t g e) -> p (i t) g e", g=NG, e=CW)
                return dve.bn_stats(stats[:, group, j, :], view[:, :, group, :])

            RECIP_LAG = 3

            def normalisation(b):
                step = [0]

                def link(ins):
                    step[0] += 1
                    ins.then_inc(norm_dve, 1)
                    dve.wait_ge(norm_dve, b * NORM_DVE + step[0])

                def by_channels(i, s):
                    link(dve.tensor_copy(by_channel[:, i], s[:, :].unsqueeze(2).broadcast_to((P, NG, CW))))

                part = stats[:, :, :, :].rearrange("p g s (h f) -> p g (s h) f", f=3)

                def sum_of_means():
                    dve.wait_ge(slab_used, (b + 1) * slabs)
                    link(dve.tensor_reduce(mean_sum[:, :], part[:, :, :, 1], AX_X, ALU.add))
                    by_channels(0, mean_sum)

                def deviations():
                    dve.wait_ge(norm_pe, b * NORM_PE + 1)
                    mean = logit_ps[:, MEAN_AT % BANKS, SPARE:SPARE + NG].unsqueeze(2).broadcast_to((P, NG, means))
                    link(dve.tensor_tensor(dev[:, :, :], part[:, :, :, 1], mean, ALU.subtract))

                def sum_of_squares():
                    dve.wait_ge(norm_pool, b * NORM_POOL + 3)
                    link(dve.tensor_reduce(spread_sum[:, :], spread[:, :, :], AX_X, ALU.add))
                    by_channels(1, spread_sum)

                def moments():
                    dve.wait_ge(norm_pe, b * NORM_PE + 2)
                    got = logit_ps[:, MOMENTS_AT % BANKS, SPARE:SPARE + 2]
                    link(dve.tensor_scalar(neg_mean[:, :], got[:, 0:1], -1.0, None, ALU.mult))
                    link(dve.tensor_scalar(var_eps[:, :], got[:, 1:2], EPS, None, ALU.add))

                def scale_rows():
                    dve.wait_ge(norm_pool, (b + 1) * NORM_POOL)
                    link(dve.tensor_scalar(M_sb[:, b % 2, :], A_sb[:, :], rstd[:, 0:1], None, ALU.mult))

                def bias():
                    dve.wait_ge(norm_pe, b * NORM_PE + 3)
                    link(dve.tensor_tensor(bias_sb[:, :], logit_ps[:, BIAS_AT % BANKS, SPARE:SPARE + K],
                                           bias_c[:, :], ALU.add))

                return {MEAN_AT - 2: sum_of_means, MEAN_AT: deviations, MOMENTS_AT - 2: sum_of_squares,
                        MOMENTS_AT: moments, MOMENTS_AT + 1: scale_rows, BIAS_AT: bias}

            def shift(n, k, first=None):
                g = n * BODY + k
                dve.wait_ge(logits_ready, done(g))
                if first is not None:
                    first()
                if k >= RECIP_LAG:
                    reciprocal(n, k - RECIP_LAG)
                for t in range(TILES):
                    own = tile(logit_ps, k % BANKS, t)
                    last = dve.tensor_tensor_reduce(own, own, bias_sb[:, :], 1.0, LOWEST, ALU.add, ALU.max,
                                                    top[:, k % RING, t:t + 1])
                last.then_inc(maxed, 1)
                dve.wait_ge(maxed, done(g))
                dve.wait_ge(logits_turned, done(g - RING))
                dve.tensor_tensor(shift_sb[:, k % RING, :].rearrange("p (t k) -> p t k", t=TILES),
                                  logit_ps[:, k % BANKS, 0:TILES * K].rearrange("p (t k) -> p t k", t=TILES),
                                  top[:, k % RING, :].unsqueeze(2).broadcast_to((P, TILES, K)),
                                  ALU.subtract).then_inc(shifted, 1)

            def reciprocal(n, k):
                g = n * BODY + k
                dve.wait_ge(mixed, done(g))
                dve.wait_ge(scaled, done(g - RING))
                sums = mix_ps[:, k % BANKS, 0:TILES * W1].rearrange("p (t c) -> p t c", t=TILES)[:, :, C]
                dve.reciprocal(rsum[:, k % RING, :], sums).then_inc(recips, 1)

            stats_at = [0] + [j * GROUP_CHUNK * SLAB_CHUNKS + REFILL_LAG for j in range(1, RESIDENT)]
            even_from = RESIDENT * GROUP_CHUNK * SLAB_CHUNKS + REFILL_LAG
            stats_end = (bodies - 1) * BODY + MEAN_AT - 2 - RECIP_LAG
            stats_at += [even_from + (stats_end - even_from) * i // (slabs - RESIDENT)
                         for i in range(slabs - RESIDENT + 1)]

            def stages(b, it, ahead):
                norm = normalisation(b + 1) if ahead and it == bodies - 1 else {}

                def statistics(_, k):
                    at = it * BODY + (k - RECIP_LAG)
                    if at >= stats_end:
                        return
                    j = max(i for i in range(slabs) if stats_at[i] <= at)
                    begin, span = stats_at[j], stats_at[j + 1] - stats_at[j]
                    if at == begin:
                        dve.wait_ge(slab_loaded[j % SLAB_BUFS], slab_landed(b + 1, j))
                    for group in range((at - begin) * NG // span, (at - begin + 1) * NG // span):
                        last = slab_stats(j % SLAB_BUFS, j, group)
                        if group == NG - 1:
                            last.then_inc(slab_used, 1)

                def shift_and_norm(n, k):
                    short = k in (MOMENTS_AT, BIAS_AT)
                    shift(n, k, norm.get(k) if short else None)
                    if k in norm and not short:
                        norm[k]()

                return [(shift_and_norm, 0)] + ([(statistics, 0)] if ahead else [])

            with dve.Fori(0, slabs // SLAB_BUFS) as h:
                for buf in range(SLAB_BUFS):
                    dve.wait_ge(slab_loaded[buf], 16 * SLAB_CHUNKS * (h + 1))
                    for group in range(NG):
                        last = slab_stats(buf, h * SLAB_BUFS + buf, group)
                    last.then_inc(slab_used, 1)
            for f in normalisation(0).values():
                f()
            all_batches(dve, RECIP_LAG, bodies - 1, stages, [(reciprocal, RECIP_LAG)])

        @block.tensor
        def _(pe):
            pe.wait_ge(consts_loaded, 16 * 5)
            pe.wait_ge(pool_const, 5)
            pe.wait_ge(vec_const, 1)
            pe.transpose(xT_ps[:, 0, 0:P], Wk_sb[:, :], ident[:, :])
            pe.transpose(xT_ps[:, 0, P:2 * P], pat_aug[:, 0:C], ident[:, :]).then_inc(set_pe, 1)
            pe.wait_ge(set_dve, 2)
            pe.matmul(logit_ps[:, 0, 0:K], WkT_sb[:, :], patT_sb[:, :], start=True, stop=True).then_inc(set_pe, 1)
            pe.wait_ge(set_dve, 3)
            pe.matmul(turn_ps[:, 0, 0:K], Wq_sb[:, :], patkT_sb[:, :], start=True, stop=True)
            pe.matmul(turn_ps[:, 0, K:2 * K], bq_sb[:, :].broadcast_to((P, P)), patkT_sb[:, :],
                      start=True, stop=True).then_inc(set_pe, 1)
            pe.wait_ge(set_dve, 5)

            def norm_product(b, k):
                if k == MEAN_AT:
                    pe.wait_ge(norm_dve, b * NORM_DVE + 1)
                    pe.matmul(logit_ps[:, k % BANKS, SPARE:SPARE + NG], mean_w[:, :], mean_sum[:, :],
                              start=True, stop=True).then_inc(norm_pe, 1)
                if k == MEAN_AT + BANKS:
                    pe.wait_ge(norm_dve, b * NORM_DVE + 3)
                if k == MOMENTS_AT:
                    pe.wait_ge(norm_dve, b * NORM_DVE + 5)
                    for i in range(2):
                        last = pe.matmul(logit_ps[:, k % BANKS, SPARE + i:SPARE + i + 1],
                                         by_channel[:, i].rearrange("p g e -> p (g e)"),
                                         mean_w[:, 0:1], start=True, stop=True)
                    last.then_inc(norm_pe, 1)
                if k == BIAS_AT:
                    pe.wait_ge(norm_dve, b * NORM_DVE + 8)
                    pe.matmul(logit_ps[:, k % BANKS, SPARE:SPARE + K], neg_mean[:, :].broadcast_to((P, P)),
                              M_sb[:, b % 2, :], start=True, stop=True).then_inc(norm_pe, 1)

            def turn_x(n, k, b, it):
                g = n * BODY + k
                if k >= BODY:
                    k -= BODY
                    b, it = (b + 1, 0) if isinstance(it, int) and it == bodies - 1 else (b, it + 1)
                if first_chunk(it) == RES_CHUNKS and k % GROUP_CHUNK == 0:
                    pe.wait_ge(x_loaded[k // GROUP_CHUNK], (b * (bodies - RES_BODIES) + (it - (RES_BODIES - 1))) * 16)
                pe.wait_ge(x_cols, done(g - BANKS))
                x_now = x_columns(it, k)
                for t in range(TILES):
                    last = pe.transpose(tile(xT_ps, k % BANKS, t), x_now[:, t * C:(t + 1) * C], ident[:, :])
                last.then_inc(x_turned, 1)

            def logits(n, k, b, next_batch=None):
                g = n * BODY + k
                pe.wait_ge(x_cols, done(g))
                pe.wait_ge(shifted, done(g - BANKS))
                if next_batch is not None:
                    norm_product(next_batch, k)
                for t in range(TILES):
                    last = pe.matmul(tile(logit_ps, k % BANKS, t), tile(xT_sb, k % RING, t), M_sb[:, b % 2, :],
                                     start=True, stop=True)
                last.then_inc(logits_ready, 1)

            def turn_logits(n, k):
                g = n * BODY + k
                pe.wait_ge(shifted, done(g))
                pe.wait_ge(probs, done(g - BANKS))
                for t in range(TILES):
                    last = pe.transpose(tile(turn_ps, k % BANKS, t), tile(shift_sb, k % RING, t), ident[:, :])
                last.then_inc(logits_turned, 1)

            def mix(n, k):
                g = n * BODY + k
                pe.wait_ge(probs, done(g))
                pe.wait_ge(scaled, done(g - BANKS))
                for t in range(TILES):
                    last = pe.matmul(tile(mix_ps, k % BANKS, t, W1, W1), tile(prob_sb, k % RING, t), pat_aug[:, :],
                                     start=True, stop=True)
                last.then_inc(mixed, 1)

            def stages(b, it, ahead):
                carried = b + 1 if ahead and isinstance(it, int) and it == bodies - 1 else None
                return [(lambda n, k: turn_x(n, k, b, it), 0), (lambda n, k: logits(n, k, batch_at(b, it, k), carried), 1),
                        (turn_logits, 2), (mix, 3)]

            for k in (MEAN_AT, MOMENTS_AT, BIAS_AT):
                norm_product(0, k)
            pe.wait_ge(norm_dve, NORM_DVE)
            all_batches(pe, 3, RES_BODIES, stages)


_INS = ['x', 'L0_conv_pattern', 'L0_conv_Wq', 'L0_conv_bq', 'L0_conv_Wk', 'L0_conv_bk']
_OUTS = [((8, 200, 288, 128), 'float32')]


def kernel(**inputs):
    import numpy as _np
    import concourse.bacc as _bacc
    from concourse import mybir as _mybir
    from concourse.bass_utils import run_bass_kernel_spmd as _run

    nc = _bacc.Bacc("TRN2", target_bir_lowering=False, num_devices=1)
    arrays, args = {}, []
    for name in _INS:
        a = _np.ascontiguousarray(inputs[name])
        arrays[f"in_{name}_dram"] = a
        args.append(nc.dram_tensor(f"in_{name}_dram", a.shape, _mybir.dt.from_np(a.dtype), kind="ExternalInput").ap())
    for i, (shape, dtype) in enumerate(_OUTS):
        dt = _mybir.dt.from_np(_np.dtype(dtype))
        args.append(nc.dram_tensor(f"out_{i}_dram", shape, dt, kind="ExternalOutput").ap())
    program(nc, *args)
    r = _run(nc, [arrays], core_ids=[0])
    got = tuple(r.results[0][f"out_{i}_dram"] for i in range(len(_OUTS)))
    return got[0]
```
